# Optimizing a Trainium2 kernel written in Bass

```python
import numpy as np
import jax
import jax.numpy as jnp

def _softmax(x, axis=-1):
    return jax.nn.softmax(x, axis=axis)

def _gelu(x):
    return jax.nn.gelu(x, approximate=True)

def _silu(x):
    return jax.nn.silu(x)

def _sigmoid(x):
    return jax.nn.sigmoid(x)

def _layernorm(x, axis=-1, eps=1e-05):
    m = jnp.mean(x, axis=axis, keepdims=True)
    v = jnp.var(x, axis=axis, keepdims=True)
    return (x - m) / jnp.sqrt(v + eps)

def _scatter_add(tgt, idx, src, axis=0):
    return tgt.at[idx].add(src)

def _segment_sum(src, seg, n):
    return jax.ops.segment_sum(src, seg, n)
kernel_name = 'mk_cond_resid_d2_seqx_r2_a4591e'

def setup_inputs(seed: int=0):
    np.random.seed(seed)
    _w = jnp.asarray

    def _rec_inputs():
        import jax
        import jax.numpy as jnp
        _rk = jax.random.key(seed)
        x = -7.109e-05 + 0.9999 * jax.random.normal(jax.random.fold_in(_rk, 1), (8, 512, 2048), jnp.float32)
        _lenS = 512 - jax.random.randint(jax.random.fold_in(_rk, 7), (8,), 0, max(1, 512 // 4) + 1, jnp.int32)
        _lenS2 = 512 - jax.random.randint(jax.random.fold_in(_rk, 8), (8,), 0, max(1, 512 // 4) + 1, jnp.int32)
        itok_B_0_15 = jax.random.randint(jax.random.fold_in(_rk, 11), (8,), 0, 16, jnp.int32)
        itok_B_9_3973 = jax.random.randint(jax.random.fold_in(_rk, 12), (8,), 9, 1987, jnp.int32)
        return (x, itok_B_0_15, itok_B_9_3973)
    x, itok_B_0_15, itok_B_9_3973 = _rec_inputs()

    def _L0_cond_setup():
        import jax, jax.numpy as jnp
        import numpy as np
        MAX_LORAS = 16
        IN, OUT = (2048, 2048)
        B, S = (8, 1024)
        key = jax.random.key(seed)
        k1, k2, k3 = jax.random.split(key, 3)
        x = jax.random.normal(k1, (B, S, IN), dtype=jnp.float32)
        adapter_ids = jax.random.randint(k2, (B,), 0, MAX_LORAS)
        weight = jax.random.normal(k3, (MAX_LORAS, OUT, IN), dtype=jnp.float32) * 0.02
        return {'x': x, 'adapter_ids': adapter_ids, 'weight': weight}
    _L0_cond_all = _L0_cond_setup()
    _L0_cond_in = {k: v for k, v in _L0_cond_all.items() if k in ('weight',)}
    del _L0_cond_all

    def _L1_cond_setup():
        import jax, jax.numpy as jnp
        import numpy as np
        from jax import lax
        B, E, T = (32, 256, 2048)
        K = 5
        PAD = (K - 1) // 2
        key = jax.random.key(seed)
        k1, k2, k3 = jax.random.split(key, 3)
        x = jax.random.normal(k1, (B, E, T), dtype=jnp.float32)
        length = jax.random.randint(k2, (B,), 1, T + 1, dtype=jnp.int64)
        conv_w = jax.random.normal(k3, (1, 1, K), dtype=jnp.float32) * (1.0 / np.sqrt(K))
        return {'x': x, 'length': length, 'conv_w': conv_w}
    _L1_cond_all = _L1_cond_setup()
    _L1_cond_in = {k: v for k, v in _L1_cond_all.items() if k in ('conv_w',)}
    del _L1_cond_all
    return {'x': x, 'itok_B_0_15': itok_B_0_15, 'itok_B_9_3973': itok_B_9_3973, 'L0_cond_weight': _L0_cond_in['weight'], 'L1_cond_conv_w': _L1_cond_in['conv_w']}

def reference(x, itok_B_0_15, itok_B_9_3973, L0_cond_weight, L1_cond_conv_w):
    import jax
    import jax.numpy as jnp

    def _L0_cond_ref(x, adapter_ids, weight):
        import jax, jax.numpy as jnp
        import numpy as np
        MAX_LORAS = 16
        IN, OUT = (2048, 2048)
        B, S = (8, 1024)
        w = weight[adapter_ids]
        return jnp.einsum('bsi,boi->bso', x, w)

    def _L1_cond_ref(x, length, conv_w):
        import jax, jax.numpy as jnp
        import numpy as np
        from jax import lax
        B, E, T = (32, 256, 2048)
        K = 5
        PAD = (K - 1) // 2
        mask = (jnp.arange(T)[None, :] < length[:, None]).astype(x.dtype)
        denom = length.astype(x.dtype)[:, None]
        y = jnp.einsum('bet,bt->be', x, mask) / denom
        yc = lax.conv_general_dilated(y[:, None, :], conv_w, window_strides=(1,), padding=[(PAD, PAD)], dimension_numbers=('NCH', 'OIH', 'NCH'))[:, 0, :]
        gate = jax.nn.sigmoid(yc)
        return x * gate[:, :, None]
    x = x + _L0_cond_ref(x, itok_B_0_15, L0_cond_weight)
    x = x + _L1_cond_ref(x, itok_B_9_3973, L1_cond_conv_w)
    return x

_drawn_inputs = setup_inputs


def setup_inputs(seed=0):
    import zlib

    import numpy as np

    out = dict(_drawn_inputs(seed))
    spreads = {}
    factors = {'L1_cond_conv_w': 4.09}
    for name, (base, spread) in spreads.items():
        noise = np.random.default_rng([zlib.crc32(name.encode()), seed]).standard_normal(out[name].shape)
        drawn = base * np.exp(spread * noise) if base else spread * noise
        out[name] = jnp.asarray(drawn.astype(out[name].dtype))
    for name, factor in factors.items():
        out[name] = (out[name] * factor).astype(out[name].dtype)
    return out
```

```python
from contextlib import ExitStack

import concourse.bass as bass
from concourse import mybir

ALU = mybir.AluOpType
ACT = mybir.ActivationFunctionType
AX_X = mybir.AxisListType.X
F32 = mybir.dt.float32
F32R = mybir.dt.float32r
BF16 = mybir.dt.bfloat16
I32 = mybir.dt.int32

P = 128
BLK = 32
QUADS = P // BLK
ROWS = 512


def lora_gate_program(nc, x, adapter_ids, lengths, weight, conv_w, out):
    B, S, D = x.shape
    ADAPTERS, OUT_DIM, _ = weight.shape
    TAPS = conv_w.shape[-1]
    PAD = (TAPS - 1) // 2
    assert S == ROWS and OUT_DIM == D and D % (QUADS * BLK) == 0

    CHUNKS = OUT_DIM // ROWS
    ST = S // P
    SLICES = D // P
    SLAB = 2
    SLABS = SLICES // SLAB
    PIECES = 2
    PSLABS = SLABS // PIECES
    PCOLS = D // QUADS // PIECES
    RB = ROWS // BLK
    SETS = 2
    OPERANDS = CHUNKS + 1
    LOAD_INC = 16 * QUADS

    x_v = x.rearrange("n (c b) (q g i) -> n q g b c i", b=BLK, q=QUADS, g=PIECES)
    w_v = weight.rearrange("a (m c b) (q g i) -> a m q g b c i", m=CHUNKS, b=BLK, q=QUADS, g=PIECES)
    res_v = x.rearrange("n (t p) (m j) -> n m p t j", p=P, m=CHUNKS)
    out_v = out.rearrange("n (t p) (m j) -> n m p t j", p=P, m=CHUNKS)

    with ExitStack() as ctx:
        def sb(name, shape, dt=F32):
            return ctx.enter_context(nc.sbuf_tensor(name, shape, dt))

        def sem(name):
            return ctx.enter_context(nc.semaphore(name))

        raw = [sb(f"raw{i}", [P, RB, PCOLS]) for i in range(2)]
        x_hi = sb("x_hi", [P, SLICES, ROWS], F32R)
        x_lo = sb("x_lo", [P, SLICES, ROWS], F32R)
        w_hi = sb("w_hi", [P, SLICES, ROWS], F32R)
        w_lo = sb("w_lo", [P, SLICES, ROWS], F32R)
        turned = [sb(f"turned{i}", [P, SLAB, ROWS]) for i in range(2)]
        x1 = sb("x1", [P, ST, D])
        column = sb("column", [P, ROWS])
        masked = [sb(f"masked{i}", [P, ROWS], BF16) for i in range(2)]
        band = sb("band", [P, 3, P])
        ids = sb("ids", [1, B], I32)
        len_i = sb("len_i", [P, B], I32)
        len_f = sb("len_f", [P, CHUNKS, B])
        len_inv = sb("len_inv", [P, B])
        taps = sb("taps", [P, TAPS])
        part = sb("part", [P, ST, CHUNKS])
        total = sb("total", [P, ST])
        mean = sb("mean", [P, ST + 2])
        gate = sb("gate", [P, ST])
        gate1 = sb("gate1", [P, ST])
        psum = ctx.enter_context(nc.psum_tensor("psum", [P, SETS, ST, ROWS], F32))

        consts_loaded = sem("consts_loaded")
        ids_loaded = sem("ids_loaded")
        raw_loaded = [sem(f"raw_loaded{i}") for i in range(2)]
        raw_turned = [sem(f"raw_turned{i}") for i in range(2)]
        x_hi_ready = sem("x_hi_ready")
        w_hi_ready = sem("w_hi_ready")
        x_lo_ready = sem("x_lo_ready")
        w_lo_ready = sem("w_lo_ready")
        slab_used = sem("slab_used")
        sums_ready = sem("sums_ready")
        set_free = [sem(f"set_free{i}") for i in range(SETS)]
        residual_loaded = [sem(f"residual_loaded{m}") for m in range(CHUNKS)]
        added = sem("added")
        summed = sem("summed")
        total_ready = sem("total_ready")
        mean_ready = sem("mean_ready")
        conv_ready = sem("conv_ready")
        gate_read = sem("gate_read")
        gate_ready = sem("gate_ready")
        scaled = sem("scaled")
        stored = [sem(f"stored{m}") for m in range(CHUNKS)]
        iota_ready = sem("iota_ready")
        band_steps = sem("band_steps")
        setup_steps = sem("setup_steps")

        block = ctx.enter_context(nc.Block())

        def x_piece(g):
            return 2 * g

        def w_piece(m, g):
            return 2 * g + 1 if m == 0 else 2 * PIECES + (m - 1) * PIECES + g

        def before(b, n):
            return OPERANDS * PIECES // 2 * b + n // 2

        @block.sync
        def _(sp):
            sp.dma_start(ids[:, :], adapter_ids.rearrange("(a n) -> a n", a=1)).then_inc(ids_loaded, 16)
            sp.wait_ge(ids_loaded, 16)

            def load(b, n, source, wait=True):
                if wait:
                    sp.wait_ge(raw_turned[n % 2], PSLABS * before(b, n))
                for q in range(QUADS):
                    sp.dma_start(raw[n % 2][BLK * q:BLK * (q + 1)], source(q)).then_inc(raw_loaded[n % 2], 16)

            def load_x(b, g, wait=True):
                load(b, x_piece(g), lambda q: x_v[bass.ds(b, 1), q, g].rearrange("n b c i -> (n b) c i"), wait)

            def load_w(b, adapter, m, g, wait=True):
                load(b, w_piece(m, g),
                     lambda q: w_v[bass.ds(adapter, 1), m, q, g].rearrange("n b c i -> (n b) c i"), wait)

            def adapter_of(b):
                return sp.value_load(ids[0:1, bass.ds(b, 1)], min_val=0, max_val=ADAPTERS - 1)

            def chunks(b, adapter, ms):
                for m in ms:
                    for g in range(PIECES):
                        load_w(b, adapter, m, g)

            def start_batch(b, first=False):
                adapter = adapter_of(b)
                for g in range(PIECES):
                    load_x(b, g, not first or g > 0)
                    load_w(b, adapter, 0, g, not first or g > 0)
                chunks(b, adapter, [1])
                for m in range(CHUNKS):
                    if not first:
                        sp.wait_ge(stored[m], b * 16)
                    sp.dma_start(x1[:, :, m * ROWS:(m + 1) * ROWS],
                                 res_v[bass.ds(b, 1), m].rearrange("n p t j -> (n p) t j")
                                 ).then_inc(residual_loaded[m], 16)

            start_batch(0, first=True)
            with sp.Fori(0, B - 1) as b:
                chunks(b, adapter_of(b), range(2, CHUNKS))
                start_batch(b + 1)
            chunks(B - 1, adapter_of(B - 1), range(2, CHUNKS))
            for m in range(CHUNKS):
                sp.wait_ge(stored[m], B * 16)

        def slab(t, k):
            return t[:, k * SLAB:(k + 1) * SLAB, :]

        @block.vector
        def _(dve):
            step = [0]

            def chain(ins, s=setup_steps):
                step[0] += 1
                ins.then_inc(s, 1)
                dve.wait_ge(s, step[0])

            dve.wait_ge(consts_loaded, 32)
            chain(nc.vector.memset(mean[:, :], 0.0))
            chain(nc.vector.tensor_copy(len_f[:, 0, :], len_i[:, :]))
            chain(nc.vector.reciprocal(len_inv[:, :], len_f[:, 0, :]))
            for m in range(1, CHUNKS):
                chain(nc.vector.tensor_scalar(len_f[:, m, :], len_f[:, 0, :], -float(m * ROWS), None, ALU.add))
            dve.wait_ge(iota_ready, 2)
            distance = turned[0][:, 0, 0:3 * P].rearrange("p (n m) -> p n m", n=3)
            term = turned[1][:, 0, 0:3 * P].rearrange("p (n m) -> p n m", n=3)
            chain(nc.vector.tensor_scalar(band[:, :, :], distance, 0.0, taps[:, 0:1], ALU.is_equal, ALU.mult))
            for j in range(1, TAPS):
                chain(nc.vector.tensor_scalar(term, distance, float(j), taps[:, j:j + 1], ALU.is_equal, ALU.mult))
                chain(nc.vector.tensor_tensor(band[:, :, :], band[:, :, :], term, ALU.add))

            def turn(b, n, t, to):
                src = raw[n % 2][:, :, t * SLAB * BLK:(t + 1) * SLAB * BLK]
                dve.wait_ge(raw_loaded[n % 2], LOAD_INC * (before(b, n) + 1))
                nc.vector.transpose(to[:, :, :].rearrange("p j (c b) -> p j c b", b=BLK),
                                    src.rearrange("p c (j a) -> p j c a", a=BLK)).then_inc(raw_turned[n % 2], 1)

            def turn_chunk(b, m):
                for k in range(SLABS):
                    done = (b * CHUNKS + m) * SLABS + k
                    dve.wait_ge(slab_used, done - SLABS + 1)
                    dve.wait_ge(w_lo_ready, done - 1)
                    if m == 1 and k == 0:
                        dve.wait_ge(x_lo_ready, (b + 1) * SLABS)
                    turn(b, w_piece(m, k // PSLABS), k % PSLABS, turned[k % 2])

            def turn_first(b, first=False):
                for k in range(SLABS):
                    done = b * CHUNKS * SLABS + k
                    if not first:
                        dve.wait_ge(slab_used, done - SLABS + 1)
                        if k == 0:
                            dve.wait_ge(w_lo_ready, done - 1)
                    if k > 0:
                        dve.wait_ge(x_lo_ready, b * SLABS + k)
                    turn(b, x_piece(k // PSLABS), k % PSLABS, turned[0])
                    if not first or k > 0:
                        dve.wait_ge(w_lo_ready, done)
                    turn(b, w_piece(0, k // PSLABS), k % PSLABS, turned[1])
                    dve.wait_ge(x_hi_ready, b * SLABS + k + 1)
                    nc.vector.tensor_tensor(slab(x_lo, k), turned[0][:, :, :], slab(x_hi, k).bitcast(F32),
                                            ALU.subtract).then_inc(x_lo_ready, 1)

            def finish_chunk(b, m):
                n = b * CHUNKS + m
                cols = slice(m * ROWS, (m + 1) * ROWS)
                dve.wait_ge(residual_loaded[m], (b + 1) * 16)
                for t in range(ST + 1):
                    if t < ST:
                        if t < ST - 1:
                            dve.wait_ge(sums_ready, n * (ST - 1) + t + 1)
                        else:
                            dve.wait_ge(slab_used, (n + 1) * SLABS)
                        nc.vector.tensor_tensor(x1[:, t, cols], psum[:, m % SETS, t, :], x1[:, t, cols],
                                                ALU.add).then_inc(set_free[m % SETS], 1)
                    if t > 0:
                        dve.wait_ge(set_free[m % SETS], (b * (CHUNKS // SETS) + m // SETS) * ST + t)
                        if t > 2:
                            dve.wait_ge(summed, n * ST + t - 2)
                        nc.vector.scalar_tensor_tensor(
                            out=masked[t % 2][:, :], in0=column[:, :], scalar=len_f[:, m, bass.ds(b, 1)],
                            in1=x1[:, t - 1, cols], op0=ALU.is_lt, op1=ALU.mult,
                            accum_out=part[:, t - 1, m:m + 1]).then_inc(summed, 1)

            def row_means(b):
                dve.wait_ge(summed, (b + 1) * CHUNKS * ST)
                nc.vector.tensor_reduce(total[:, :], part[:, :, :], AX_X, ALU.add).then_inc(total_ready, 1)
                dve.wait_ge(total_ready, b + 1)
                nc.vector.tensor_scalar(mean[:, 1:ST + 1], total[:, :], len_inv[:, bass.ds(b, 1)], None,
                                        ALU.mult).then_inc(mean_ready, 1)

            def batch_chunks(b):
                for m in range(1, CHUNKS):
                    turn_chunk(b, m)
                    finish_chunk(b, m - 1)

            turn_first(0, first=True)
            with dve.Fori(0, B - 1) as b:
                batch_chunks(b)
                turn_first(b + 1)
                finish_chunk(b, CHUNKS - 1)
                row_means(b)
            batch_chunks(B - 1)
            finish_chunk(B - 1, CHUNKS - 1)
            row_means(B - 1)

        @block.scalar
        def _(act):
            act.dma_start(len_i[:, :], lengths.rearrange("(a n) -> a n", a=1).to_broadcast([P, B])
                          ).then_inc(consts_loaded, 16)
            act.dma_start(taps[:, :], conv_w.rearrange("a b k -> (a b) k").to_broadcast([P, TAPS])
                          ).then_inc(consts_loaded, 16)

            def round_slab(b, n, t, hi, full, ready):
                act.wait_ge(raw_turned[n % 2], PSLABS * before(b, n) + t + 1)
                nc.scalar.copy(hi, full[:, :, :]).then_inc(ready, 1)

            def round_chunk(b, m):
                for k in range(SLABS):
                    round_slab(b, w_piece(m, k // PSLABS), k % PSLABS, slab(w_hi, k), turned[k % 2], w_hi_ready)

            def round_first(b):
                for k in range(SLABS):
                    round_slab(b, x_piece(k // PSLABS), k % PSLABS, slab(x_hi, k), turned[0], x_hi_ready)
                    round_slab(b, w_piece(0, k // PSLABS), k % PSLABS, slab(w_hi, k), turned[1], w_hi_ready)

            def store(b, m):
                act.wait_ge(scaled, b * CHUNKS + m + 1)
                act.dma_start(out_v[bass.ds(b, 1), m].rearrange("n p t j -> (n p) t j"),
                              x1[:, :, m * ROWS:(m + 1) * ROWS]).then_inc(stored[m], 16)

            def gate_and_store(b):
                act.wait_ge(conv_ready, b + 1)
                nc.scalar.activation(gate[:, :], psum[:, 1, 0, 0:ST], ACT.Sigmoid).then_inc(gate_read, 1)
                act.wait_ge(gate_read, b + 1)
                nc.scalar.add(gate1[:, :], gate[:, :], 1.0).then_inc(gate_ready, 1)
                act.wait_ge(gate_ready, b + 1)
                for m in range(CHUNKS):
                    cols = slice(m * ROWS, (m + 1) * ROWS)
                    for t in range(ST):
                        last = nc.scalar.mul(x1[:, t, cols], x1[:, t, cols], gate1[:, t:t + 1])
                    last.then_inc(scaled, 1)
                    if m > 0:
                        store(b, m - 1)
                store(b, CHUNKS - 1)

            round_first(0)
            with act.Fori(0, B - 1) as b:
                for m in range(1, CHUNKS):
                    round_chunk(b, m)
                round_first(b + 1)
                gate_and_store(b)
            for m in range(1, CHUNKS):
                round_chunk(B - 1, m)
            gate_and_store(B - 1)

        @block.gpsimd
        def _(pool):
            for n, shift in enumerate((0, -P, P)):
                last = nc.gpsimd.iota(turned[0][:, 0, n * P:(n + 1) * P], pattern=[[-1, P]], base=shift + PAD,
                                      channel_multiplier=1, allow_small_or_imprecise_dtypes=True)
            last.then_inc(iota_ready, 1)
            nc.gpsimd.iota(column[:, :], pattern=[[1, ROWS]], base=0, channel_multiplier=0,
                           allow_small_or_imprecise_dtypes=True).then_inc(iota_ready, 1)

            def split_chunk(b, m):
                for k in range(SLABS):
                    pool.wait_ge(w_hi_ready, (b * CHUNKS + m) * SLABS + k + 1)
                    full = turned[1 if m == 0 else k % 2]
                    nc.gpsimd.tensor_tensor(slab(w_lo, k), full[:, :, :], slab(w_hi, k).bitcast(F32),
                                            ALU.subtract).then_inc(w_lo_ready, 1)

            with pool.Fori(0, B) as b:
                for m in range(CHUNKS):
                    split_chunk(b, m)

        @block.tensor
        def _(pe):
            def multiply_slab(b, m, k):
                pe.wait_ge(w_lo_ready, (b * CHUNKS + m) * SLABS + k + 1)
                if m == 0:
                    pe.wait_ge(x_lo_ready, b * SLABS + k + 1)
                for s in range(k * SLAB, (k + 1) * SLAB):
                    for t in range(ST):
                        acc = psum[:, m % SETS, t, :]
                        rows = slice(t * P, (t + 1) * P)
                        last_slice = s == SLICES - 1
                        nc.tensor.matmul(acc, x_hi[:, s, rows], w_hi[:, s, :], start=(s == 0), stop=False)
                        nc.tensor.matmul(acc, x_hi[:, s, rows], w_lo[:, s, :], start=False, stop=False)
                        mm = nc.tensor.matmul(acc, x_lo[:, s, rows], w_hi[:, s, :], start=False, stop=last_slice)
                        if last_slice and t < ST - 1:
                            mm.then_inc(sums_ready, 1)
                mm.then_inc(slab_used, 1)

            def convolve(b):
                acc = psum[:, 1, 0, 0:ST]
                pe.wait_ge(mean_ready, b + 1)
                nc.tensor.matmul(acc, band[:, 0, :], mean[:, 1:ST + 1], start=True, stop=False)
                nc.tensor.matmul(acc, band[:, 1, :], mean[:, 0:ST], start=False, stop=False)
                nc.tensor.matmul(acc, band[:, 2, :], mean[:, 2:ST + 2], start=False, stop=True).then_inc(conv_ready, 1)

            def chunk(b, m, first=False, conv_of=None):
                if not first:
                    pe.wait_ge(set_free[m % SETS], (b * (CHUNKS // SETS) + m // SETS) * ST)
                    if m == 1:
                        pe.wait_ge(gate_ready, b)
                for k in range(SLABS):
                    multiply_slab(b, m, k)
                    if conv_of is not None and k == 1:
                        convolve(conv_of)

            for m in range(SETS):
                chunk(0, m, first=True)
            with pe.Fori(0, B - 1) as b:
                for m in range(SETS, CHUNKS):
                    chunk(b, m)
                chunk(b + 1, 0, conv_of=b)
                chunk(b + 1, 1)
            for m in range(SETS, CHUNKS):
                chunk(B - 1, m)
            convolve(B - 1)


def kernel(x, itok_B_0_15, itok_B_9_3973, L0_cond_weight, L1_cond_conv_w):
    import numpy as np
    import concourse.bacc as bacc
    from concourse.bass_utils import run_bass_kernel_spmd

    arrays = {
        "x": np.ascontiguousarray(x),
        "adapter_ids": np.ascontiguousarray(itok_B_0_15),
        "lengths": np.ascontiguousarray(itok_B_9_3973),
        "weight": np.ascontiguousarray(L0_cond_weight),
        "conv_w": np.ascontiguousarray(L1_cond_conv_w),
    }
    nc = bacc.Bacc("TRN2", target_bir_lowering=False, num_devices=1)
    aps = {name: nc.dram_tensor(name, a.shape, mybir.dt.from_np(a.dtype), kind="ExternalInput").ap()
           for name, a in arrays.items()}
    out = nc.dram_tensor("out", arrays["x"].shape, F32, kind="ExternalOutput").ap()
    lora_gate_program(nc, aps["x"], aps["adapter_ids"], aps["lengths"], aps["weight"], aps["conv_w"], out)
    r = run_bass_kernel_spmd(nc, [arrays], core_ids=[0])
    return r.results[0]["out"]
```

```python
from contextlib import ExitStack

import concourse.bass as bass
from concourse import mybir

ALU = mybir.AluOpType
ACT = mybir.ActivationFunctionType
AX_X = mybir.AxisListType.X
F32 = mybir.dt.float32
F32R = mybir.dt.float32r
BF16 = mybir.dt.bfloat16
I32 = mybir.dt.int32

P = 128
BLK = 32
QUADS = P // BLK
ROWS = 512


def lora_gate_program(nc, x, adapter_ids, lengths, weight, conv_w, out):
    B, S, D = x.shape
    ADAPTERS, OUT_DIM, _ = weight.shape
    TAPS = conv_w.shape[-1]
    PAD = (TAPS - 1) // 2
    assert S == ROWS and OUT_DIM == D and D % (QUADS * BLK) == 0

    CHUNKS = OUT_DIM // ROWS
    ST = S // P
    SLICES = D // P
    PIECES = 2
    PSLICES = SLICES // PIECES
    PCOLS = D // QUADS // PIECES
    LAST = 2
    TURNED = 4
    RB = ROWS // BLK
    SETS = 2
    OPERANDS = CHUNKS + 1
    LOAD_INC = 16 * QUADS

    x_v = x.rearrange("n (c b) (q g i) -> n q g b c i", b=BLK, q=QUADS, g=PIECES)
    w_v = weight.rearrange("a (m c b) (q g i) -> a m q g b c i", m=CHUNKS, b=BLK, q=QUADS, g=PIECES)
    res_v = x.rearrange("n (t p) (m j) -> n m p t j", p=P, m=CHUNKS)
    out_v = out.rearrange("n (t p) (m j) -> n m p t j", p=P, m=CHUNKS)

    with ExitStack() as ctx:
        def sb(name, shape, dt=F32):
            return ctx.enter_context(nc.sbuf_tensor(name, shape, dt))

        def sem(name):
            return ctx.enter_context(nc.semaphore(name))

        raw = [sb(f"raw{i}", [P, RB, PCOLS]) for i in range(2)]
        x_hi = sb("x_hi", [P, SLICES, ROWS], F32R)
        x_lo = sb("x_lo", [P, SLICES, ROWS], F32R)
        w_hi = sb("w_hi", [P, SLICES, ROWS], F32R)
        w_lo = sb("w_lo", [P, SLICES, ROWS], F32R)
        turned = [sb(f"turned{i}", [P, ROWS]) for i in range(TURNED)]
        x1 = sb("x1", [P, ST, D])
        column = sb("column", [P, ROWS])
        masked = sb("masked", [P, 2, ROWS], BF16)
        distance = sb("distance", [P, 3, P])
        band = sb("band", [P, 3, P])
        ids = sb("ids", [1, B], I32)
        len_i = sb("len_i", [P, B], I32)
        len_f = sb("len_f", [P, CHUNKS, B])
        len_inv = sb("len_inv", [P, B])
        taps = sb("taps", [P, TAPS])
        part = sb("part", [P, ST, CHUNKS])
        total = sb("total", [P, ST])
        mean = sb("mean", [P, ST + 2])
        gate = sb("gate", [P, ST])
        gate1 = sb("gate1", [P, ST])
        psum = ctx.enter_context(nc.psum_tensor("psum", [P, SETS, ST, ROWS], F32))

        consts_loaded = sem("consts_loaded")
        ids_loaded = sem("ids_loaded")
        raw_loaded = [sem(f"raw_loaded{i}") for i in range(2)]
        half_loaded = [sem(f"half_loaded{i}") for i in range(2)]
        raw_turned = [sem(f"raw_turned{i}") for i in range(2)]
        x_hi_ready = sem("x_hi_ready")
        w_hi_ready = sem("w_hi_ready")
        x_lo_ready = sem("x_lo_ready")
        w_lo_ready = sem("w_lo_ready")
        slice_used = sem("slice_used")
        sums_ready = sem("sums_ready")
        set_free = [sem(f"set_free{i}") for i in range(SETS)]
        residual_loaded = [sem(f"residual_loaded{m}") for m in range(CHUNKS)]
        added = sem("added")
        summed = sem("summed")
        total_ready = sem("total_ready")
        mean_ready = sem("mean_ready")
        conv_ready = sem("conv_ready")
        gate_read = sem("gate_read")
        gate_ready = sem("gate_ready")
        scaled = sem("scaled")
        stored = [sem(f"stored{m}") for m in range(CHUNKS)]
        iota_ready = sem("iota_ready")
        band_steps = sem("band_steps")
        setup_steps = sem("setup_steps")

        block = ctx.enter_context(nc.Block())

        def x_piece(g):
            return 2 * g

        def w_piece(m, g):
            return 2 * g + 1 if m == 0 else 2 * PIECES + (m - 1) * PIECES + g

        def before(b, n):
            return OPERANDS * PIECES // 2 * b + n // 2

        @block.sync
        def _(sp):
            sp.dma_start(ids[:, :], adapter_ids.rearrange("(a n) -> a n", a=1)).then_inc(ids_loaded, 16)

            def load(b, n, source):
                sp.wait_ge(raw_turned[n % 2], PSLICES * before(b, n))
                for q in range(QUADS):
                    sp.dma_start(raw[n % 2][BLK * q:BLK * (q + 1)],
                                 source(q).rearrange("n b c i -> (n b) c i")).then_inc(raw_loaded[n % 2], 16)

            def load_half(n, half, source):
                if n >= 2:
                    sp.wait_ge(raw_turned[n % 2], PSLICES * (before(0, n) - 1) + PSLICES // 2 * (half + 1))
                cols = slice(half * PCOLS // 2, (half + 1) * PCOLS // 2)
                for q in range(QUADS):
                    sp.dma_start(raw[n % 2][BLK * q:BLK * (q + 1), :, cols],
                                 source(q)[:, :, :, cols].rearrange("n b c i -> (n b) c i")
                                 ).then_inc((raw_loaded if half else half_loaded)[n % 2], 16)

            def x_at(b, g):
                return lambda q: x_v[bass.ds(b, 1), q, g]

            def w_at(adapter, m, g):
                return lambda q: w_v[bass.ds(adapter, 1), m, q, g]

            def adapter_of(b):
                return sp.value_load(ids[0:1, bass.ds(b, 1)], min_val=0, max_val=ADAPTERS - 1)

            def chunks(b, adapter, ms):
                for m in ms:
                    for g in range(PIECES):
                        load(b, w_piece(m, g), w_at(adapter, m, g))

            def start_batch(b, adapter, first=False):
                if not first:
                    for g in range(PIECES):
                        load(b, x_piece(g), x_at(b, g))
                        load(b, w_piece(0, g), w_at(adapter, 0, g))
                chunks(b, adapter, [1])
                for m in range(CHUNKS):
                    if not first:
                        sp.wait_ge(stored[m], b * 16)
                    sp.dma_start(x1[:, :, m * ROWS:(m + 1) * ROWS],
                                 res_v[bass.ds(b, 1), m].rearrange("n p t j -> (n p) t j")
                                 ).then_inc(residual_loaded[m], 16)

            load_half(x_piece(0), 0, x_at(0, 0))
            sp.wait_ge(ids_loaded, 16)
            adapter = adapter_of(0)
            load_half(w_piece(0, 0), 0, w_at(adapter, 0, 0))
            load_half(x_piece(0), 1, x_at(0, 0))
            load_half(w_piece(0, 0), 1, w_at(adapter, 0, 0))
            for g in range(1, PIECES):
                for half in range(2):
                    load_half(x_piece(g), half, x_at(0, g))
                    load_half(w_piece(0, g), half, w_at(adapter, 0, g))
            start_batch(0, adapter, first=True)
            with sp.Fori(0, B - 1) as b:
                chunks(b, adapter_of(b), range(2, CHUNKS))
                start_batch(b + 1, adapter_of(b + 1))
            chunks(B - 1, adapter_of(B - 1), range(2, CHUNKS))
            for m in range(CHUNKS):
                sp.wait_ge(stored[m], B * 16)

        def turned_x(k):
            return turned[2 * (k % 2)]

        def turned_w(m, k):
            return turned[2 * (k % 2) + 1] if m == 0 else turned[k % TURNED]

        @block.vector
        def _(dve):
            step = [0]

            def chain(ins):
                step[0] += 1
                ins.then_inc(setup_steps, 1)
                dve.wait_ge(setup_steps, step[0])

            def prepare_lengths():
                dve.wait_ge(consts_loaded, 32)
                chain(nc.vector.memset(mean[:, :], 0.0))
                chain(nc.vector.tensor_copy(len_f[:, 0, :], len_i[:, :]))
                chain(nc.vector.reciprocal(len_inv[:, :], len_f[:, 0, :]))
                for m in range(1, CHUNKS):
                    chain(nc.vector.tensor_scalar(len_f[:, m, :], len_f[:, 0, :], -float(m * ROWS), None, ALU.add))

            def prepare_band():
                term = masked[:, :, :].rearrange("p a r -> p (a r)").bitcast(F32)[:, 0:3 * P]
                term = term.rearrange("p (n m) -> p n m", n=3)
                dve.wait_ge(iota_ready, 2)
                chain(nc.vector.tensor_scalar(band[:, :, :], distance[:, :, :], 0.0, taps[:, 0:1],
                                              ALU.is_equal, ALU.mult))
                for j in range(1, TAPS):
                    chain(nc.vector.tensor_scalar(term, distance[:, :, :], float(j), taps[:, j:j + 1],
                                                  ALU.is_equal, ALU.mult))
                    chain(nc.vector.tensor_tensor(band[:, :, :], band[:, :, :], term, ALU.add))

            def turn(b, n, t, to, halved=False):
                if halved and t < PSLICES // 2:
                    dve.wait_ge(half_loaded[n % 2], LOAD_INC * (before(b, n) + 1))
                else:
                    dve.wait_ge(raw_loaded[n % 2], LOAD_INC * (before(b, n) + 1))
                nc.vector.transpose(to[:, :].rearrange("p (c b) -> p c b", b=BLK),
                                    raw[n % 2][:, :, t * BLK:(t + 1) * BLK]).then_inc(raw_turned[n % 2], 1)

            def turn_chunk(b, m):
                for k in range(SLICES):
                    done = (b * CHUNKS + m) * SLICES + k
                    dve.wait_ge(slice_used, done - SLICES + 1)
                    dve.wait_ge(w_lo_ready, done - 2)
                    if m == 1 and k == 0:
                        dve.wait_ge(x_lo_ready, (b + 1) * SLICES)
                    turn(b, w_piece(m, k // PSLICES), k % PSLICES, turned_w(m, k))

            def turn_first(b, first=False):
                def split_x(k):
                    dve.wait_ge(x_hi_ready, b * SLICES + k + 1)
                    nc.vector.tensor_tensor(x_lo[:, k, :], turned_x(k)[:, :], x_hi[:, k, :].bitcast(F32),
                                            ALU.subtract).then_inc(x_lo_ready, 1)

                for k in range(SLICES):
                    done = b * CHUNKS * SLICES + k
                    if not first:
                        dve.wait_ge(slice_used, done - SLICES + 1)
                    if not first or k > 1:
                        dve.wait_ge(w_lo_ready, done - 1)
                    if k > 1:
                        dve.wait_ge(x_lo_ready, b * SLICES + k - 1)
                    turn(b, x_piece(k // PSLICES), k % PSLICES, turned_x(k), first)
                    turn(b, w_piece(0, k // PSLICES), k % PSLICES, turned_w(0, k), first)
                    if k > 0:
                        split_x(k - 1)
                split_x(SLICES - 1)

            def finish_chunk(b, m):
                n = b * CHUNKS + m
                cols = slice(m * ROWS, (m + 1) * ROWS)
                dve.wait_ge(residual_loaded[m], (b + 1) * 16)
                for t in range(ST + 1):
                    if t < ST:
                        if t < ST - 1:
                            dve.wait_ge(sums_ready, n * (ST - 1) + t + 1)
                        else:
                            dve.wait_ge(slice_used, (n + 1) * SLICES)
                        nc.vector.tensor_tensor(x1[:, t, cols], psum[:, m % SETS, t, :], x1[:, t, cols],
                                                ALU.add).then_inc(set_free[m % SETS], 1)
                    if t > 0:
                        dve.wait_ge(set_free[m % SETS], (b * (CHUNKS // SETS) + m // SETS) * ST + t)
                        if t > 2:
                            dve.wait_ge(summed, n * ST + t - 2)
                        nc.vector.scalar_tensor_tensor(
                            out=masked[:, t % 2, :], in0=column[:, :], scalar=len_f[:, m, bass.ds(b, 1)],
                            in1=x1[:, t - 1, cols], op0=ALU.is_lt, op1=ALU.mult,
                            accum_out=part[:, t - 1, m:m + 1]).then_inc(summed, 1)

            def row_means(b):
                dve.wait_ge(summed, (b + 1) * CHUNKS * ST)
                nc.vector.tensor_reduce(total[:, :], part[:, :, :], AX_X, ALU.add).then_inc(total_ready, 1)
                dve.wait_ge(total_ready, b + 1)
                nc.vector.tensor_scalar(mean[:, 1:ST + 1], total[:, :], len_inv[:, bass.ds(b, 1)], None,
                                        ALU.mult).then_inc(mean_ready, 1)

            def batch_chunks(b):
                for m in range(1, CHUNKS):
                    turn_chunk(b, m)
                    finish_chunk(b, m - 1)

            turn_first(0, first=True)
            prepare_lengths()
            prepare_band()
            with dve.Fori(0, B - 1) as b:
                batch_chunks(b)
                turn_first(b + 1)
                finish_chunk(b, CHUNKS - 1)
                row_means(b)
            batch_chunks(B - 1)
            finish_chunk(B - 1, CHUNKS - 1)
            row_means(B - 1)

        @block.scalar
        def _(act):
            act.dma_start(len_i[:, :], lengths.rearrange("(a n) -> a n", a=1).to_broadcast([P, B])
                          ).then_inc(consts_loaded, 16)
            act.dma_start(taps[:, :], conv_w.rearrange("a b k -> (a b) k").to_broadcast([P, TAPS])
                          ).then_inc(consts_loaded, 16)

            def round_slice(b, n, t, hi, full, ready):
                act.wait_ge(raw_turned[n % 2], PSLICES * before(b, n) + t + 1)
                nc.scalar.copy(hi, full[:, :]).then_inc(ready, 1)

            def round_w(b, m, k):
                round_slice(b, w_piece(m, k // PSLICES), k % PSLICES, w_hi[:, k, :], turned_w(m, k), w_hi_ready)

            def round_chunk(b, m):
                for k in range(SLICES):
                    round_w(b, m, k)

            def round_first(b):
                for k in range(SLICES):
                    round_slice(b, x_piece(k // PSLICES), k % PSLICES, x_hi[:, k, :], turned_x(k), x_hi_ready)
                    round_w(b, 0, k)

            def store(b, m):
                act.wait_ge(scaled, b * CHUNKS + m + 1)
                act.dma_start(out_v[bass.ds(b, 1), m].rearrange("n p t j -> (n p) t j"),
                              x1[:, :, m * ROWS:(m + 1) * ROWS]).then_inc(stored[m], 16)

            def gate_and_store(b):
                act.wait_ge(conv_ready, b + 1)
                nc.scalar.activation(gate[:, :], psum[:, 1, 0, 0:ST], ACT.Sigmoid).then_inc(gate_read, 1)
                act.wait_ge(gate_read, b + 1)
                nc.scalar.add(gate1[:, :], gate[:, :], 1.0).then_inc(gate_ready, 1)
                act.wait_ge(gate_ready, b + 1)
                for m in range(CHUNKS):
                    cols = slice(m * ROWS, (m + 1) * ROWS)
                    for t in range(ST):
                        last = nc.scalar.mul(x1[:, t, cols], x1[:, t, cols], gate1[:, t:t + 1])
                    last.then_inc(scaled, 1)
                    if m > 0:
                        store(b, m - 1)
                store(b, CHUNKS - 1)

            round_first(0)
            with act.Fori(0, B - 1) as b:
                for m in range(1, CHUNKS):
                    round_chunk(b, m)
                round_first(b + 1)
                gate_and_store(b)
            for m in range(1, CHUNKS):
                round_chunk(B - 1, m)
            gate_and_store(B - 1)

        @block.gpsimd
        def _(pool):
            for n, shift in enumerate((0, -P, P)):
                last = nc.gpsimd.iota(distance[:, n, :], pattern=[[-1, P]], base=shift + PAD,
                                      channel_multiplier=1, allow_small_or_imprecise_dtypes=True)
            last.then_inc(iota_ready, 1)
            nc.gpsimd.iota(column[:, :], pattern=[[1, ROWS]], base=0, channel_multiplier=0,
                           allow_small_or_imprecise_dtypes=True).then_inc(iota_ready, 1)

            def split_chunk(b, m):
                for k in range(SLICES):
                    pool.wait_ge(w_hi_ready, (b * CHUNKS + m) * SLICES + k + 1)
                    nc.gpsimd.tensor_tensor(w_lo[:, k, :], turned_w(m, k)[:, :], w_hi[:, k, :].bitcast(F32),
                                            ALU.subtract).then_inc(w_lo_ready, 1)

            with pool.Fori(0, B) as b:
                for m in range(CHUNKS):
                    split_chunk(b, m)

        @block.tensor
        def _(pe):
            def multiply(b, m, ks):
                for t in range(ST):
                    for k in ks:
                        if t == 0:
                            pe.wait_ge(w_lo_ready, (b * CHUNKS + m) * SLICES + k + 1)
                            if m == 0:
                                pe.wait_ge(x_lo_ready, b * SLICES + k + 1)
                        mm = three_passes(m, k, t)
                        if t == ST - 1:
                            mm.then_inc(slice_used, 1)
                        elif k == SLICES - 1:
                            mm.then_inc(sums_ready, 1)

            def three_passes(m, k, t):
                acc = psum[:, m % SETS, t, :]
                rows = slice(t * P, (t + 1) * P)
                nc.tensor.matmul(acc, x_hi[:, k, rows], w_hi[:, k, :], start=(k == 0), stop=False)
                nc.tensor.matmul(acc, x_hi[:, k, rows], w_lo[:, k, :], start=False, stop=False)
                return nc.tensor.matmul(acc, x_lo[:, k, rows], w_hi[:, k, :], start=False, stop=(k == SLICES - 1))

            def convolve(b):
                acc = psum[:, 1, 0, 0:ST]
                pe.wait_ge(mean_ready, b + 1)
                nc.tensor.matmul(acc, band[:, 0, :], mean[:, 1:ST + 1], start=True, stop=False)
                nc.tensor.matmul(acc, band[:, 1, :], mean[:, 0:ST], start=False, stop=False)
                nc.tensor.matmul(acc, band[:, 2, :], mean[:, 2:ST + 2], start=False, stop=True).then_inc(conv_ready, 1)

            def chunk(b, m, first=False, conv_of=None):
                if not first:
                    pe.wait_ge(set_free[m % SETS], (b * (CHUNKS // SETS) + m // SETS) * ST)
                    if m == 1:
                        pe.wait_ge(gate_ready, b)
                for k in range(SLICES - LAST):
                    if conv_of is not None and k == SLICES // 2:
                        convolve(conv_of)
                    multiply(b, m, [k])
                multiply(b, m, range(SLICES - LAST, SLICES))

            for m in range(SETS):
                chunk(0, m, first=True)
            with pe.Fori(0, B - 1) as b:
                for m in range(SETS, CHUNKS):
                    chunk(b, m)
                chunk(b + 1, 0, conv_of=b)
                chunk(b + 1, 1)
            for m in range(SETS, CHUNKS):
                chunk(B - 1, m)
            convolve(B - 1)


def kernel(x, itok_B_0_15, itok_B_9_3973, L0_cond_weight, L1_cond_conv_w):
    import numpy as np
    import concourse.bacc as bacc
    from concourse.bass_utils import run_bass_kernel_spmd

    arrays = {
        "x": np.ascontiguousarray(x),
        "adapter_ids": np.ascontiguousarray(itok_B_0_15),
        "lengths": np.ascontiguousarray(itok_B_9_3973),
        "weight": np.ascontiguousarray(L0_cond_weight),
        "conv_w": np.ascontiguousarray(L1_cond_conv_w),
    }
    nc = bacc.Bacc("TRN2", target_bir_lowering=False, num_devices=1)
    aps = {name: nc.dram_tensor(name, a.shape, mybir.dt.from_np(a.dtype), kind="ExternalInput").ap()
           for name, a in arrays.items()}
    out = nc.dram_tensor("out", arrays["x"].shape, F32, kind="ExternalOutput").ap()
    lora_gate_program(nc, aps["x"], aps["adapter_ids"], aps["lengths"], aps["weight"], aps["conv_w"], out)
    r = run_bass_kernel_spmd(nc, [arrays], core_ids=[0])
    return r.results[0]["out"]
```

```python
from contextlib import ExitStack

import concourse.bass as bass
from concourse import mybir

ALU = mybir.AluOpType
ACT = mybir.ActivationFunctionType
AX_X = mybir.AxisListType.X
F32 = mybir.dt.float32
F32R = mybir.dt.float32r
BF16 = mybir.dt.bfloat16
I32 = mybir.dt.int32

P = 128
BLK = 32
QUADS = P // BLK
ROWS = 512


def lora_gate_program(nc, x, adapter_ids, lengths, weight, conv_w, out):
    B, S, D = x.shape
    ADAPTERS, OUT_DIM, _ = weight.shape
    TAPS = conv_w.shape[-1]
    PAD = (TAPS - 1) // 2
    assert S == ROWS and OUT_DIM == D and D % (QUADS * BLK) == 0

    CHUNKS = OUT_DIM // ROWS
    ST = S // P
    SLICES = D // P
    PIECES = 2
    PSLICES = SLICES // PIECES
    PCOLS = D // QUADS // PIECES
    LAST = 2
    TURNED = 4
    RB = ROWS // BLK
    SETS = 2
    OPERANDS = CHUNKS + 1
    LOAD_INC = 16 * QUADS

    x_v = x.rearrange("n (c b) (q g i) -> n q g b c i", b=BLK, q=QUADS, g=PIECES)
    w_v = weight.rearrange("a (m c b) (q g i) -> a m q g b c i", m=CHUNKS, b=BLK, q=QUADS, g=PIECES)
    res_v = x.rearrange("n (t p) (m j) -> n m p t j", p=P, m=CHUNKS)
    out_v = out.rearrange("n (t p) (m j) -> n m p t j", p=P, m=CHUNKS)
    out_tile = out.rearrange("n (t p) d -> n t p d", p=P)

    with ExitStack() as ctx:
        def sb(name, shape, dt=F32):
            return ctx.enter_context(nc.sbuf_tensor(name, shape, dt))

        def sem(name):
            return ctx.enter_context(nc.semaphore(name))

        raw = [sb(f"raw{i}", [P, RB, PCOLS]) for i in range(2)]
        x_hi = sb("x_hi", [P, SLICES, ROWS], F32R)
        x_lo = sb("x_lo", [P, SLICES, ROWS], F32R)
        w_hi = sb("w_hi", [P, SLICES, ROWS], F32R)
        w_lo = sb("w_lo", [P, SLICES, ROWS], F32R)
        turned = [sb(f"turned{i}", [P, ROWS]) for i in range(TURNED)]
        x1 = sb("x1", [P, ST, D])
        column = sb("column", [P, ROWS])
        masked = sb("masked", [P, 2, ROWS], BF16)
        distance = sb("distance", [P, 3, P])
        band = sb("band", [P, 3, P])
        ids = sb("ids", [1, B], I32)
        len_i = sb("len_i", [P, B], I32)
        len_f = sb("len_f", [P, CHUNKS, B])
        len_inv = sb("len_inv", [P, B])
        taps = sb("taps", [P, TAPS])
        part = sb("part", [P, ST, CHUNKS])
        total = sb("total", [P, ST])
        mean = sb("mean", [P, ST + 2])
        gate = sb("gate", [P, ST])
        gate1 = sb("gate1", [P, ST])
        psum = ctx.enter_context(nc.psum_tensor("psum", [P, SETS, ST, ROWS], F32))

        consts_loaded = sem("consts_loaded")
        ids_loaded = sem("ids_loaded")
        raw_loaded = [sem(f"raw_loaded{i}") for i in range(2)]
        half_loaded = [sem(f"half_loaded{i}") for i in range(2)]
        raw_turned = [sem(f"raw_turned{i}") for i in range(2)]
        x_hi_ready = sem("x_hi_ready")
        w_hi_ready = sem("w_hi_ready")
        x_lo_ready = sem("x_lo_ready")
        w_lo_ready = sem("w_lo_ready")
        slice_used = sem("slice_used")
        sums_ready = sem("sums_ready")
        set_free = [sem(f"set_free{i}") for i in range(SETS)]
        residual_loaded = [sem(f"residual_loaded{m}") for m in range(CHUNKS)]
        summed = sem("summed")
        total_ready = sem("total_ready")
        mean_ready = sem("mean_ready")
        conv_ready = sem("conv_ready")
        gate_read = sem("gate_read")
        gate_ready = sem("gate_ready")
        scaled = sem("scaled")
        stored = [sem(f"stored{m}") for m in range(CHUNKS)]
        tile_mean_ready = sem("tile_mean_ready")
        tile_conv_ready = sem("tile_conv_ready")
        tile_gate_read = sem("tile_gate_read")
        tile_gate_ready = sem("tile_gate_ready")
        tile_scaled = sem("tile_scaled")
        last_tile_scaled = sem("last_tile_scaled")
        tile_stored = sem("tile_stored")
        iota_ready = sem("iota_ready")
        setup_steps = sem("setup_steps")

        block = ctx.enter_context(nc.Block())

        LAST_TILES = [range(t, t + 1) for t in range(ST - 2)] + [range(ST - 2, ST)]

        def tile_conv(i):
            return psum[:, 0, i, LAST_TILES[i].start:LAST_TILES[i].stop]

        def x_piece(g):
            return 2 * g

        def w_piece(m, g):
            return 2 * g + 1 if m == 0 else 2 * PIECES + (m - 1) * PIECES + g

        def before(b, n):
            return OPERANDS * PIECES // 2 * b + n // 2

        @block.sync
        def _(sp):
            sp.dma_start(ids[:, :], adapter_ids.rearrange("(a n) -> a n", a=1)).then_inc(ids_loaded, 16)

            def load(b, n, source):
                sp.wait_ge(raw_turned[n % 2], PSLICES * before(b, n))
                for q in range(QUADS):
                    sp.dma_start(raw[n % 2][BLK * q:BLK * (q + 1)],
                                 source(q).rearrange("n b c i -> (n b) c i")).then_inc(raw_loaded[n % 2], 16)

            def load_half(n, half, source):
                if n >= 2:
                    sp.wait_ge(raw_turned[n % 2], PSLICES * (before(0, n) - 1) + PSLICES // 2 * (half + 1))
                cols = slice(half * PCOLS // 2, (half + 1) * PCOLS // 2)
                for q in range(QUADS):
                    sp.dma_start(raw[n % 2][BLK * q:BLK * (q + 1), :, cols],
                                 source(q)[:, :, :, cols].rearrange("n b c i -> (n b) c i")
                                 ).then_inc((raw_loaded if half else half_loaded)[n % 2], 16)

            def x_at(b, g):
                return lambda q: x_v[bass.ds(b, 1), q, g]

            def w_at(adapter, m, g):
                return lambda q: w_v[bass.ds(adapter, 1), m, q, g]

            def adapter_of(b):
                return sp.value_load(ids[0:1, bass.ds(b, 1)], min_val=0, max_val=ADAPTERS - 1)

            def chunks(b, adapter, ms):
                for m in ms:
                    for g in range(PIECES):
                        load(b, w_piece(m, g), w_at(adapter, m, g))

            def start_batch(b, adapter, first=False):
                if not first:
                    for g in range(PIECES):
                        load(b, x_piece(g), x_at(b, g))
                        load(b, w_piece(0, g), w_at(adapter, 0, g))
                chunks(b, adapter, [1])
                for m in range(CHUNKS):
                    if not first:
                        sp.wait_ge(stored[m], b * 16)
                    sp.dma_start(x1[:, :, m * ROWS:(m + 1) * ROWS],
                                 res_v[bass.ds(b, 1), m].rearrange("n p t j -> (n p) t j")
                                 ).then_inc(residual_loaded[m], 16)

            load_half(x_piece(0), 0, x_at(0, 0))
            sp.wait_ge(ids_loaded, 16)
            adapter = adapter_of(0)
            load_half(w_piece(0, 0), 0, w_at(adapter, 0, 0))
            load_half(x_piece(0), 1, x_at(0, 0))
            load_half(w_piece(0, 0), 1, w_at(adapter, 0, 0))
            for g in range(1, PIECES):
                for half in range(2):
                    load_half(x_piece(g), half, x_at(0, g))
                    load_half(w_piece(0, g), half, w_at(adapter, 0, g))
            start_batch(0, adapter, first=True)
            with sp.Fori(0, B - 1) as b:
                chunks(b, adapter_of(b), range(2, CHUNKS))
                start_batch(b + 1, adapter_of(b + 1))
            chunks(B - 1, adapter_of(B - 1), range(2, CHUNKS))
            sp.wait_ge(last_tile_scaled, 1)
            sp.dma_start(out_tile[B - 1, ST - 1], x1[:, ST - 1, :]).then_inc(tile_stored, 16)
            for m in range(CHUNKS):
                sp.wait_ge(stored[m], (B - 1) * 16)
            sp.wait_ge(tile_stored, ST * 16)

        def turned_x(k):
            return turned[2 * (k % 2)]

        def turned_w(m, k):
            return turned[2 * (k % 2) + 1] if m == 0 else turned[k % TURNED]

        @block.vector
        def _(dve):
            step = [0]

            def chain(ins):
                step[0] += 1
                ins.then_inc(setup_steps, 1)
                dve.wait_ge(setup_steps, step[0])

            def prepare_lengths():
                dve.wait_ge(consts_loaded, 32)
                chain(nc.vector.memset(mean[:, :], 0.0))
                chain(nc.vector.tensor_copy(len_f[:, 0, :], len_i[:, :]))
                chain(nc.vector.reciprocal(len_inv[:, :], len_f[:, 0, :]))
                for m in range(1, CHUNKS):
                    chain(nc.vector.tensor_scalar(len_f[:, m, :], len_f[:, 0, :], -float(m * ROWS), None, ALU.add))

            def prepare_band():
                term = masked[:, :, :].rearrange("p a r -> p (a r)").bitcast(F32)[:, 0:3 * P]
                term = term.rearrange("p (n m) -> p n m", n=3)
                dve.wait_ge(iota_ready, 2)
                chain(nc.vector.tensor_scalar(band[:, :, :], distance[:, :, :], 0.0, taps[:, 0:1],
                                              ALU.is_equal, ALU.mult))
                for j in range(1, TAPS):
                    chain(nc.vector.tensor_scalar(term, distance[:, :, :], float(j), taps[:, j:j + 1],
                                                  ALU.is_equal, ALU.mult))
                    chain(nc.vector.tensor_tensor(band[:, :, :], band[:, :, :], term, ALU.add))

            def turn(b, n, t, to, halved=False):
                if halved and t < PSLICES // 2:
                    dve.wait_ge(half_loaded[n % 2], LOAD_INC * (before(b, n) + 1))
                else:
                    dve.wait_ge(raw_loaded[n % 2], LOAD_INC * (before(b, n) + 1))
                nc.vector.transpose(to[:, :].rearrange("p (c b) -> p c b", b=BLK),
                                    raw[n % 2][:, :, t * BLK:(t + 1) * BLK]).then_inc(raw_turned[n % 2], 1)

            def turn_chunk(b, m):
                for k in range(SLICES):
                    done = (b * CHUNKS + m) * SLICES + k
                    dve.wait_ge(slice_used, done - SLICES + 1)
                    dve.wait_ge(w_lo_ready, done - 2)
                    if m == 1 and k == 0:
                        dve.wait_ge(x_lo_ready, (b + 1) * SLICES)
                    turn(b, w_piece(m, k // PSLICES), k % PSLICES, turned_w(m, k))

            def turn_first(b, first=False):
                def split_x(k):
                    dve.wait_ge(x_hi_ready, b * SLICES + k + 1)
                    nc.vector.tensor_tensor(x_lo[:, k, :], turned_x(k)[:, :], x_hi[:, k, :].bitcast(F32),
                                            ALU.subtract).then_inc(x_lo_ready, 1)

                for k in range(SLICES):
                    done = b * CHUNKS * SLICES + k
                    if not first:
                        dve.wait_ge(slice_used, done - SLICES + 1)
                    if not first or k > 1:
                        dve.wait_ge(w_lo_ready, done - 1)
                    if k > 1:
                        dve.wait_ge(x_lo_ready, b * SLICES + k - 1)
                    turn(b, x_piece(k // PSLICES), k % PSLICES, turned_x(k), first)
                    turn(b, w_piece(0, k // PSLICES), k % PSLICES, turned_w(0, k), first)
                    if k > 0:
                        split_x(k - 1)
                split_x(SLICES - 1)

            def add_product(b, m, t):
                n = b * CHUNKS + m
                cols = slice(m * ROWS, (m + 1) * ROWS)
                if t < ST - 1:
                    dve.wait_ge(sums_ready, n * (ST - 1) + t + 1)
                else:
                    dve.wait_ge(slice_used, (n + 1) * SLICES)
                nc.vector.tensor_tensor(x1[:, t, cols], psum[:, m % SETS, t, :], x1[:, t, cols],
                                        ALU.add).then_inc(set_free[m % SETS], 1)

            def masked_sum(b, m, t):
                n = b * CHUNKS + m
                dve.wait_ge(set_free[m % SETS], (b * (CHUNKS // SETS) + m // SETS) * ST + t + 1)
                if t > 1:
                    dve.wait_ge(summed, n * ST + t - 1)
                nc.vector.scalar_tensor_tensor(
                    out=masked[:, t % 2, :], in0=column[:, :], scalar=len_f[:, m, bass.ds(b, 1)],
                    in1=x1[:, t, m * ROWS:(m + 1) * ROWS], op0=ALU.is_lt, op1=ALU.mult,
                    accum_out=part[:, t, m:m + 1]).then_inc(summed, 1)

            def finish_chunk(b, m):
                dve.wait_ge(residual_loaded[m], (b + 1) * 16)
                add_product(b, m, 0)
                for t in range(1, ST):
                    add_product(b, m, t)
                    masked_sum(b, m, t - 1)
                masked_sum(b, m, ST - 1)

            def row_means(b):
                dve.wait_ge(summed, (b + 1) * CHUNKS * ST)
                nc.vector.tensor_reduce(total[:, :], part[:, :, :], AX_X, ALU.add).then_inc(total_ready, 1)
                dve.wait_ge(total_ready, b + 1)
                nc.vector.tensor_scalar(mean[:, 1:ST + 1], total[:, :], len_inv[:, bass.ds(b, 1)], None,
                                        ALU.mult).then_inc(mean_ready, 1)

            def finish_by_tile(b, m):
                dve.wait_ge(residual_loaded[m], (b + 1) * 16)
                for t in range(ST):
                    add_product(b, m, t)
                    masked_sum(b, m, t)
                    dve.wait_ge(summed, (b * CHUNKS + m) * ST + t + 1)
                    nc.vector.tensor_reduce(total[:, t:t + 1], part[:, t, :], AX_X, ALU.add).then_inc(total_ready, 1)
                    dve.wait_ge(total_ready, b + t + 1)
                    nc.vector.tensor_scalar(mean[:, t + 1:t + 2], total[:, t:t + 1], len_inv[:, b:b + 1], None,
                                            ALU.mult).then_inc(tile_mean_ready, 1)
                dve.wait_ge(tile_gate_ready, len(LAST_TILES))
                nc.vector.tensor_scalar(x1[:, ST - 1, :], x1[:, ST - 1, :], gate1[:, ST - 1:ST], None,
                                        ALU.mult).then_inc(last_tile_scaled, 1)

            def batch_chunks(b):
                for m in range(1, CHUNKS):
                    turn_chunk(b, m)
                    finish_chunk(b, m - 1)

            turn_first(0, first=True)
            prepare_lengths()
            prepare_band()
            with dve.Fori(0, B - 1) as b:
                batch_chunks(b)
                turn_first(b + 1)
                finish_chunk(b, CHUNKS - 1)
                row_means(b)
            batch_chunks(B - 1)
            finish_by_tile(B - 1, CHUNKS - 1)

        @block.scalar
        def _(act):
            act.dma_start(len_i[:, :], lengths.rearrange("(a n) -> a n", a=1).to_broadcast([P, B])
                          ).then_inc(consts_loaded, 16)
            act.dma_start(taps[:, :], conv_w.rearrange("a b k -> (a b) k").to_broadcast([P, TAPS])
                          ).then_inc(consts_loaded, 16)

            def round_slice(b, n, t, hi, full, ready):
                act.wait_ge(raw_turned[n % 2], PSLICES * before(b, n) + t + 1)
                nc.scalar.copy(hi, full[:, :]).then_inc(ready, 1)

            def round_w(b, m, k):
                round_slice(b, w_piece(m, k // PSLICES), k % PSLICES, w_hi[:, k, :], turned_w(m, k), w_hi_ready)

            def round_chunk(b, m):
                for k in range(SLICES):
                    round_w(b, m, k)

            def round_first(b):
                for k in range(SLICES):
                    round_slice(b, x_piece(k // PSLICES), k % PSLICES, x_hi[:, k, :], turned_x(k), x_hi_ready)
                    round_w(b, 0, k)

            def store(b, m):
                act.wait_ge(scaled, b * CHUNKS + m + 1)
                act.dma_start(out_v[bass.ds(b, 1), m].rearrange("n p t j -> (n p) t j"),
                              x1[:, :, m * ROWS:(m + 1) * ROWS]).then_inc(stored[m], 16)

            def gate_and_store(b):
                act.wait_ge(conv_ready, b + 1)
                nc.scalar.activation(gate[:, :], psum[:, 1, 0, 0:ST], ACT.Sigmoid).then_inc(gate_read, 1)
                act.wait_ge(gate_read, b + 1)
                nc.scalar.add(gate1[:, :], gate[:, :], 1.0).then_inc(gate_ready, 1)
                act.wait_ge(gate_ready, b + 1)
                for m in range(CHUNKS):
                    cols = slice(m * ROWS, (m + 1) * ROWS)
                    for t in range(ST):
                        last = nc.scalar.mul(x1[:, t, cols], x1[:, t, cols], gate1[:, t:t + 1])
                    last.then_inc(scaled, 1)
                    if m > 0:
                        store(b, m - 1)
                store(b, CHUNKS - 1)

            round_first(0)
            with act.Fori(0, B - 1) as b:
                for m in range(1, CHUNKS):
                    round_chunk(b, m)
                round_first(b + 1)
                gate_and_store(b)
            for m in range(1, CHUNKS):
                round_chunk(B - 1, m)
            for i, tiles in enumerate(LAST_TILES):
                act.wait_ge(tile_conv_ready, i + 1)
                nc.scalar.activation(gate[:, tiles.start:tiles.stop], tile_conv(i), ACT.Sigmoid
                                     ).then_inc(tile_gate_read, 1)
                act.wait_ge(tile_gate_read, i + 1)
                nc.scalar.add(gate1[:, tiles.start:tiles.stop], gate[:, tiles.start:tiles.stop], 1.0
                              ).then_inc(tile_gate_ready, 1)
                act.wait_ge(tile_gate_ready, i + 1)
                t = tiles.start
                nc.scalar.mul(x1[:, t, :], x1[:, t, :], gate1[:, t:t + 1]).then_inc(tile_scaled, 1)
                act.wait_ge(tile_scaled, i + 1)
                act.dma_start(out_tile[B - 1, t], x1[:, t, :]).then_inc(tile_stored, 16)

        @block.gpsimd
        def _(pool):
            for n, shift in enumerate((0, -P, P)):
                last = nc.gpsimd.iota(distance[:, n, :], pattern=[[-1, P]], base=shift + PAD,
                                      channel_multiplier=1, allow_small_or_imprecise_dtypes=True)
            last.then_inc(iota_ready, 1)
            nc.gpsimd.iota(column[:, :], pattern=[[1, ROWS]], base=0, channel_multiplier=0,
                           allow_small_or_imprecise_dtypes=True).then_inc(iota_ready, 1)

            def split_chunk(b, m):
                for k in range(SLICES):
                    pool.wait_ge(w_hi_ready, (b * CHUNKS + m) * SLICES + k + 1)
                    nc.gpsimd.tensor_tensor(w_lo[:, k, :], turned_w(m, k)[:, :], w_hi[:, k, :].bitcast(F32),
                                            ALU.subtract).then_inc(w_lo_ready, 1)

            with pool.Fori(0, B) as b:
                for m in range(CHUNKS):
                    split_chunk(b, m)

        @block.tensor
        def _(pe):
            def multiply(b, m, ks):
                for t in range(ST):
                    for k in ks:
                        if t == 0:
                            pe.wait_ge(w_lo_ready, (b * CHUNKS + m) * SLICES + k + 1)
                            if m == 0:
                                pe.wait_ge(x_lo_ready, b * SLICES + k + 1)
                        mm = three_passes(m, k, t)
                        if t == ST - 1:
                            mm.then_inc(slice_used, 1)
                        elif k == SLICES - 1:
                            mm.then_inc(sums_ready, 1)

            def three_passes(m, k, t):
                acc = psum[:, m % SETS, t, :]
                rows = slice(t * P, (t + 1) * P)
                nc.tensor.matmul(acc, x_hi[:, k, rows], w_hi[:, k, :], start=(k == 0), stop=False)
                nc.tensor.matmul(acc, x_hi[:, k, rows], w_lo[:, k, :], start=False, stop=False)
                return nc.tensor.matmul(acc, x_lo[:, k, rows], w_hi[:, k, :], start=False, stop=(k == SLICES - 1))

            def convolve(b):
                acc = psum[:, 1, 0, 0:ST]
                pe.wait_ge(mean_ready, b + 1)
                nc.tensor.matmul(acc, band[:, 0, :], mean[:, 1:ST + 1], start=True, stop=False)
                nc.tensor.matmul(acc, band[:, 1, :], mean[:, 0:ST], start=False, stop=False)
                nc.tensor.matmul(acc, band[:, 2, :], mean[:, 2:ST + 2], start=False, stop=True).then_inc(conv_ready, 1)

            def convolve_tiles(i):
                a, z = LAST_TILES[i].start, LAST_TILES[i].stop
                pe.wait_ge(tile_mean_ready, min(z + 1, ST))
                nc.tensor.matmul(tile_conv(i), band[:, 0, :], mean[:, a + 1:z + 1], start=True, stop=False)
                nc.tensor.matmul(tile_conv(i), band[:, 1, :], mean[:, a:z], start=False, stop=False)
                nc.tensor.matmul(tile_conv(i), band[:, 2, :], mean[:, a + 2:z + 2], start=False, stop=True
                                 ).then_inc(tile_conv_ready, 1)

            def last_chunk(b, m):
                wait_for_set(b, m)
                for t in range(ST):
                    for k in range(SLICES):
                        if t == 0:
                            pe.wait_ge(w_lo_ready, (b * CHUNKS + m) * SLICES + k + 1)
                        if t == 2 and k == SLICES // 2:
                            pe.wait_ge(set_free[0], B * CHUNKS // SETS * ST)
                        if t >= 2 and k == SLICES // 2:
                            convolve_tiles(t - 2)
                        mm = three_passes(m, k, t)
                        if t == ST - 1:
                            mm.then_inc(slice_used, 1)
                    if t < ST - 1:
                        mm.then_inc(sums_ready, 1)
                convolve_tiles(ST - 2)

            def wait_for_set(b, m):
                pe.wait_ge(set_free[m % SETS], (b * (CHUNKS // SETS) + m // SETS) * ST)

            def chunk(b, m, first=False, conv_of=None):
                if not first:
                    wait_for_set(b, m)
                    if m == 1:
                        pe.wait_ge(gate_ready, b)
                for k in range(SLICES - LAST):
                    if conv_of is not None and k == SLICES // 2:
                        convolve(conv_of)
                    multiply(b, m, [k])
                multiply(b, m, range(SLICES - LAST, SLICES))

            for m in range(SETS):
                chunk(0, m, first=True)
            with pe.Fori(0, B - 1) as b:
                for m in range(SETS, CHUNKS):
                    chunk(b, m)
                chunk(b + 1, 0, conv_of=b)
                chunk(b + 1, 1)
            for m in range(SETS, CHUNKS - 1):
                chunk(B - 1, m)
            last_chunk(B - 1, CHUNKS - 1)


def kernel(x, itok_B_0_15, itok_B_9_3973, L0_cond_weight, L1_cond_conv_w):
    import numpy as np
    import concourse.bacc as bacc
    from concourse.bass_utils import run_bass_kernel_spmd

    arrays = {
        "x": np.ascontiguousarray(x),
        "adapter_ids": np.ascontiguousarray(itok_B_0_15),
        "lengths": np.ascontiguousarray(itok_B_9_3973),
        "weight": np.ascontiguousarray(L0_cond_weight),
        "conv_w": np.ascontiguousarray(L1_cond_conv_w),
    }
    nc = bacc.Bacc("TRN2", target_bir_lowering=False, num_devices=1)
    aps = {name: nc.dram_tensor(name, a.shape, mybir.dt.from_np(a.dtype), kind="ExternalInput").ap()
           for name, a in arrays.items()}
    out = nc.dram_tensor("out", arrays["x"].shape, F32, kind="ExternalOutput").ap()
    lora_gate_program(nc, aps["x"], aps["adapter_ids"], aps["lengths"], aps["weight"], aps["conv_w"], out)
    r = run_bass_kernel_spmd(nc, [arrays], core_ids=[0])
    return r.results[0]["out"]
```
